# Optimizing a Trainium2 kernel written in Bass

```python
import numpy as np
import jax
import jax.numpy as jnp

def _softmax(x, axis=-1):
    return jax.nn.softmax(x, axis=axis)

def _gelu(x):
    return jax.nn.gelu(x, approximate=True)

def _silu(x):
    return jax.nn.silu(x)

def _sigmoid(x):
    return jax.nn.sigmoid(x)

def _layernorm(x, axis=-1, eps=1e-05):
    m = jnp.mean(x, axis=axis, keepdims=True)
    v = jnp.var(x, axis=axis, keepdims=True)
    return (x - m) / jnp.sqrt(v + eps)

def _scatter_add(tgt, idx, src, axis=0):
    return tgt.at[idx].add(src)

def _segment_sum(src, seg, n):
    return jax.ops.segment_sum(src, seg, n)
kernel_name = 'mk_dlrm_tower_d1_rec_r8_67cc8b'

def setup_inputs(seed: int=0):
    np.random.seed(seed)
    _w = jnp.asarray

    def _rec_inputs():
        import jax
        import jax.numpy as jnp
        _tk = jax.random.key(seed)
        ids = jnp.stack([jax.random.randint(jax.random.fold_in(_tk, 200 + f), (2048,), 0, v, jnp.int32) for f, v in enumerate([12500, 1250, 1000, 125000, 12500, 1000, 12500, 1250, 1000, 1250, 1000, 12500, 12500, 1250, 1250, 12500, 12500, 1250, 1250, 1250, 1250, 1250, 1250, 1000, 1250, 1250])], axis=1)
        tbl_0 = 0.05 * jax.random.normal(jax.random.fold_in(_tk, 500 + 0), (12500, 128), jnp.float32)
        tbl_1 = 0.05 * jax.random.normal(jax.random.fold_in(_tk, 500 + 1), (1250, 128), jnp.float32)
        tbl_2 = 0.05 * jax.random.normal(jax.random.fold_in(_tk, 500 + 2), (1000, 128), jnp.float32)
        tbl_3 = 0.05 * jax.random.normal(jax.random.fold_in(_tk, 500 + 3), (125000, 128), jnp.float32)
        tbl_4 = 0.05 * jax.random.normal(jax.random.fold_in(_tk, 500 + 4), (12500, 128), jnp.float32)
        tbl_5 = 0.05 * jax.random.normal(jax.random.fold_in(_tk, 500 + 5), (1000, 128), jnp.float32)
        tbl_6 = 0.05 * jax.random.normal(jax.random.fold_in(_tk, 500 + 6), (12500, 128), jnp.float32)
        tbl_7 = 0.05 * jax.random.normal(jax.random.fold_in(_tk, 500 + 7), (1250, 128), jnp.float32)
        tbl_8 = 0.05 * jax.random.normal(jax.random.fold_in(_tk, 500 + 8), (1000, 128), jnp.float32)
        tbl_9 = 0.05 * jax.random.normal(jax.random.fold_in(_tk, 500 + 9), (1250, 128), jnp.float32)
        tbl_10 = 0.05 * jax.random.normal(jax.random.fold_in(_tk, 500 + 10), (1000, 128), jnp.float32)
        tbl_11 = 0.05 * jax.random.normal(jax.random.fold_in(_tk, 500 + 11), (12500, 128), jnp.float32)
        tbl_12 = 0.05 * jax.random.normal(jax.random.fold_in(_tk, 500 + 12), (12500, 128), jnp.float32)
        tbl_13 = 0.05 * jax.random.normal(jax.random.fold_in(_tk, 500 + 13), (1250, 128), jnp.float32)
        tbl_14 = 0.05 * jax.random.normal(jax.random.fold_in(_tk, 500 + 14), (1250, 128), jnp.float32)
        tbl_15 = 0.05 * jax.random.normal(jax.random.fold_in(_tk, 500 + 15), (12500, 128), jnp.float32)
        tbl_16 = 0.05 * jax.random.normal(jax.random.fold_in(_tk, 500 + 16), (12500, 128), jnp.float32)
        tbl_17 = 0.05 * jax.random.normal(jax.random.fold_in(_tk, 500 + 17), (1250, 128), jnp.float32)
        tbl_18 = 0.05 * jax.random.normal(jax.random.fold_in(_tk, 500 + 18), (1250, 128), jnp.float32)
        tbl_19 = 0.05 * jax.random.normal(jax.random.fold_in(_tk, 500 + 19), (1250, 128), jnp.float32)
        tbl_20 = 0.05 * jax.random.normal(jax.random.fold_in(_tk, 500 + 20), (1250, 128), jnp.float32)
        tbl_21 = 0.05 * jax.random.normal(jax.random.fold_in(_tk, 500 + 21), (1250, 128), jnp.float32)
        tbl_22 = 0.05 * jax.random.normal(jax.random.fold_in(_tk, 500 + 22), (1250, 128), jnp.float32)
        tbl_23 = 0.05 * jax.random.normal(jax.random.fold_in(_tk, 500 + 23), (1000, 128), jnp.float32)
        tbl_24 = 0.05 * jax.random.normal(jax.random.fold_in(_tk, 500 + 24), (1250, 128), jnp.float32)
        tbl_25 = 0.05 * jax.random.normal(jax.random.fold_in(_tk, 500 + 25), (1250, 128), jnp.float32)
        _rk = jax.random.fold_in(_tk, 7)
        r_dense_x = -0.000514642 + 1.00011 * jax.random.normal(jax.random.fold_in(_rk, 101), (2048, 128), jnp.float32)
        W_top1 = 0.0456912 * jax.random.normal(jax.random.fold_in(_tk, 801), (479, 512), jnp.float32)
        W_top2 = 0.0441942 * jax.random.normal(jax.random.fold_in(_tk, 802), (512, 256), jnp.float32)
        W_top3 = 0.0625 * jax.random.normal(jax.random.fold_in(_tk, 803), (256, 1), jnp.float32)
        b_top1 = jnp.zeros((512,), jnp.float32)
        b_top2 = jnp.zeros((256,), jnp.float32)
        return (r_dense_x, ids, tbl_0, tbl_1, tbl_2, tbl_3, tbl_4, tbl_5, tbl_6, tbl_7, tbl_8, tbl_9, tbl_10, tbl_11, tbl_12, tbl_13, tbl_14, tbl_15, tbl_16, tbl_17, tbl_18, tbl_19, tbl_20, tbl_21, tbl_22, tbl_23, tbl_24, tbl_25, W_top1, b_top1, W_top2, b_top2, W_top3)
    r_dense_x, ids, tbl_0, tbl_1, tbl_2, tbl_3, tbl_4, tbl_5, tbl_6, tbl_7, tbl_8, tbl_9, tbl_10, tbl_11, tbl_12, tbl_13, tbl_14, tbl_15, tbl_16, tbl_17, tbl_18, tbl_19, tbl_20, tbl_21, tbl_22, tbl_23, tbl_24, tbl_25, W_top1, b_top1, W_top2, b_top2, W_top3 = _rec_inputs()

    def _L0_rec_setup():
        import jax, jax.numpy as jnp
        import numpy as np
        F = 26
        D = 128
        B = 2048
        _TRIU_I, _TRIU_J = np.triu_indices(F + 1, k=1)
        _TRIU_I = jnp.asarray(_TRIU_I)
        _TRIU_J = jnp.asarray(_TRIU_J)
        key = jax.random.key(seed)
        k1, k2 = jax.random.split(key)
        sparse_x = jax.random.normal(k1, (B, F, D), dtype=jnp.float32)
        dense_x = jax.random.normal(k2, (B, D), dtype=jnp.float32)
        return {'sparse_x': sparse_x, 'dense_x': dense_x}
    _L0_rec_all = _L0_rec_setup()
    _L0_rec_in = {k: v for k, v in _L0_rec_all.items() if k in ()}
    del _L0_rec_all
    return {'r_dense_x': r_dense_x, 'ids': ids, 'tbl_0': tbl_0, 'tbl_1': tbl_1, 'tbl_2': tbl_2, 'tbl_3': tbl_3, 'tbl_4': tbl_4, 'tbl_5': tbl_5, 'tbl_6': tbl_6, 'tbl_7': tbl_7, 'tbl_8': tbl_8, 'tbl_9': tbl_9, 'tbl_10': tbl_10, 'tbl_11': tbl_11, 'tbl_12': tbl_12, 'tbl_13': tbl_13, 'tbl_14': tbl_14, 'tbl_15': tbl_15, 'tbl_16': tbl_16, 'tbl_17': tbl_17, 'tbl_18': tbl_18, 'tbl_19': tbl_19, 'tbl_20': tbl_20, 'tbl_21': tbl_21, 'tbl_22': tbl_22, 'tbl_23': tbl_23, 'tbl_24': tbl_24, 'tbl_25': tbl_25, 'W_top1': W_top1, 'b_top1': b_top1, 'W_top2': W_top2, 'b_top2': b_top2, 'W_top3': W_top3}

def reference(r_dense_x, ids, tbl_0, tbl_1, tbl_2, tbl_3, tbl_4, tbl_5, tbl_6, tbl_7, tbl_8, tbl_9, tbl_10, tbl_11, tbl_12, tbl_13, tbl_14, tbl_15, tbl_16, tbl_17, tbl_18, tbl_19, tbl_20, tbl_21, tbl_22, tbl_23, tbl_24, tbl_25, W_top1, b_top1, W_top2, b_top2, W_top3):
    import jax
    import jax.numpy as jnp

    def _L0_rec_ref(sparse_x, dense_x):
        import jax, jax.numpy as jnp
        import numpy as np
        F = 26
        D = 128
        B = 2048
        _TRIU_I, _TRIU_J = np.triu_indices(F + 1, k=1)
        _TRIU_I = jnp.asarray(_TRIU_I)
        _TRIU_J = jnp.asarray(_TRIU_J)
        combined = jnp.concatenate([sparse_x, dense_x[:, None, :]], axis=1)
        interact = jnp.einsum('bfd,bgd->bfg', combined, combined)
        return interact[:, _TRIU_I, _TRIU_J]
    e = jnp.stack([tbl_0[ids[:, 0]], tbl_1[ids[:, 1]], tbl_2[ids[:, 2]], tbl_3[ids[:, 3]], tbl_4[ids[:, 4]], tbl_5[ids[:, 5]], tbl_6[ids[:, 6]], tbl_7[ids[:, 7]], tbl_8[ids[:, 8]], tbl_9[ids[:, 9]], tbl_10[ids[:, 10]], tbl_11[ids[:, 11]], tbl_12[ids[:, 12]], tbl_13[ids[:, 13]], tbl_14[ids[:, 14]], tbl_15[ids[:, 15]], tbl_16[ids[:, 16]], tbl_17[ids[:, 17]], tbl_18[ids[:, 18]], tbl_19[ids[:, 19]], tbl_20[ids[:, 20]], tbl_21[ids[:, 21]], tbl_22[ids[:, 22]], tbl_23[ids[:, 23]], tbl_24[ids[:, 24]], tbl_25[ids[:, 25]]], axis=1)
    z = _L0_rec_ref(e, r_dense_x)
    z = z.reshape(z.shape[0], -1)
    h = jnp.concatenate([z, r_dense_x], axis=1)
    h = jnp.maximum(h @ W_top1 + b_top1, 0.0)
    h = jnp.maximum(h @ W_top2 + b_top2, 0.0)
    y = h @ W_top3
    return y

_drawn_inputs = setup_inputs


def setup_inputs(seed=0):
    import zlib

    import numpy as np

    out = dict(_drawn_inputs(seed))
    spreads = {'b_top1': (0.0, 0.1), 'b_top2': (0.0, 0.1)}
    factors = {}
    for name, (base, spread) in spreads.items():
        noise = np.random.default_rng([zlib.crc32(name.encode()), seed]).standard_normal(out[name].shape)
        drawn = base * np.exp(spread * noise) if base else spread * noise
        out[name] = jnp.asarray(drawn.astype(out[name].dtype))
    for name, factor in factors.items():
        out[name] = (out[name] * factor).astype(out[name].dtype)
    return out
```

```python
from contextlib import ExitStack

import concourse.bass as bass
from concourse import mybir

F32 = mybir.dt.float32
I32 = mybir.dt.int32
ALU = mybir.AluOpType
ACT = mybir.ActivationFunctionType

P = 128
NF = 26
NV = NF + 1
D = 128
B = 2048
TILES = 4
CS = TILES * P
CHUNKS = B // CS
QUAD = 32
Q = P // QUAD
GROUPS = P // Q
ROUND = 8
ROUNDS = GROUPS // ROUND
PAIRS = NV * (NV - 1) // 2
KZ = 3
KP = PAIRS // KZ
H1, H2 = 512, 256
N1, N2 = H1 // P, H2 // P
TURN = 4
BATCHES = -(-NV // TURN)
PACKS = -(-NF // TURN)
PACK0, Z0, L10, L20, L30 = 0, PACKS, PACKS + KZ, PACKS + KZ + N1, PACKS + KZ + N1 + N2
USES = L30 + 1
BANK_USES = [-(-USES // 2), USES // 2]

assert KP * KZ == PAIRS and KP <= P and NV <= QUAD and D == P


def pair_start(g):
    return g * NV - g * (g + 1) // 2


def build(nc, dense, ids, tables, w1, b1, w2, b2, w3, y):
    with ExitStack() as ctx:
        def sb(name, shape, dt=F32):
            return ctx.enter_context(nc.sbuf_tensor(name, shape, dt))

        def psum(name, shape):
            return ctx.enter_context(nc.psum_tensor(name, shape, F32))

        def sem(name):
            return ctx.enter_context(nc.semaphore(name))

        idx = sb("idx", [P, TILES, NF], I32)
        rows = sb("rows", [P, 2, NV, D])
        xt = sb("xt", [P, TILES, P, QUAD])
        gram = sb("gram", [P, NF, TILES, GROUPS])
        packed = sb("packed", [P, Q, PAIRS])
        zt = sb("zt", [KP, KZ, CS])
        h1 = sb("h1", [P, N1, CS])
        h2 = sb("h2", [P, N2, CS])
        y_row = sb("y_row", [1, CS])
        w1z = sb("w1z", [KP, KZ, H1])
        w1d = sb("w1d", [P, H1])
        w2s = sb("w2s", [P, N1, H2])
        w3s = sb("w3s", [P, N2])
        b1s = sb("b1s", [P, N1])
        b2s = sb("b2s", [P, N2])
        ident = sb("ident", [P, P])

        turn_ps = psum("turn_ps", [P, 2, TURN, P])
        gram_ps = psum("gram_ps", [P, 2, ROUND, P])
        shared_ps = psum("shared_ps", [P, 2, CS])

        s_idx = [sem(f"s_idx{k}") for k in range(TILES)]
        s_gathered = [sem(f"s_gathered{s}") for s in range(2)]
        s_tile_open = sem("s_tile_open")
        s_dense = [sem(f"s_dense{s}") for s in range(2)]
        s_weights = sem("s_weights")
        s_zero = sem("s_zero")
        s_ident = sem("s_ident")
        s_pads = sem("s_pads")
        s_turned = [sem(f"s_turned{s}") for s in range(2)]
        s_xt = [sem(f"s_xt{b}") for b in range(2)]
        s_gram = [sem(f"s_gram{b}") for b in range(2)]
        s_gram_act = [sem(f"s_gram_act{b}") for b in range(2)]
        s_gram_dve = [sem(f"s_gram_dve{b}") for b in range(2)]
        s_shared = [sem(f"s_shared{b}") for b in range(2)]
        s_taken = [sem(f"s_taken{b}") for b in range(2)]
        s_y = sem("s_y")
        s_out = sem("s_out")

        def xt_columns(k, grp):
            return xt[:, k, grp * Q:(grp + 1) * Q, 0:NV]

        def xt_blocks(k, grp):
            return xt[:, k, grp * Q:(grp + 1) * Q, :].rearrange("p q f -> p (q f)")

        def batch(i):
            f = i * TURN
            return f, min(TURN, NV - f)

        def slot_tiles(c, k):
            return c * (TILES // 2) + k // 2

        def turned(c, k, n):
            return slot_tiles(c, k) * BATCHES + (n + 1)

        def bank_batches(c, u, n):
            return c * (TILES * BATCHES // 2) + (u // 2 + n + 1)

        def half_rounds(c, r):
            return c * (TILES * ROUNDS // 2) + r // 2

        def shared_uses(c, u):
            return c * BANK_USES[u % 2] + u // 2

        def taken(eng, c, u):
            for v in (u - 1, u) if u else (u,):
                eng.wait_ge(s_taken[v % 2], shared_uses(c, v) + 2)

        block = ctx.enter_context(nc.Block())

        @block.sync
        def _(sp):
            for k in range(TILES):
                sp.dma_start(idx[:, k, :], ids[k * P:(k + 1) * P, :]).then_inc(s_idx[k], 16)
            for s in range(2):
                sp.dma_start(rows[:, s, NF, :], dense[s * P:(s + 1) * P, :]).then_inc(s_dense[s], 16)
            sp.dma_start(w1z[:], w1[0:PAIRS, :].rearrange("(c p) n -> p c n", p=KP)).then_inc(s_weights, 16)
            sp.dma_start(w1d[:], w1[PAIRS:PAIRS + D, :]).then_inc(s_weights, 16)
            sp.dma_start(w2s[:], w2.rearrange("(c p) n -> p c n", p=P)).then_inc(s_weights, 16)
            with nc.allow_non_contiguous_dma(reason="small vectors, one value per partition"):
                sp.dma_start(w3s[:], w3.rearrange("(c p) o -> p (c o)", p=P)).then_inc(s_weights, 16)
                sp.dma_start(b1s[:], b1.rearrange("(c p) -> p c", p=P)).then_inc(s_weights, 16)
                sp.dma_start(b2s[:], b2.rearrange("(c p) -> p c", p=P)).then_inc(s_weights, 16)
            with sp.Fori(0, CHUNKS - 1) as c:
                for k in range(TILES):
                    sp.wait_ge(s_gathered[k % 2], (slot_tiles(c, k) + 1) * (16 * NF))
                    sp.dma_start(idx[:, k, :], ids[bass.ds((c + 1) * CS + k * P, P), :]).then_inc(s_idx[k], 16)
                    sp.wait_ge(s_turned[k % 2], turned(c, k, BATCHES))
                    sp.dma_start(rows[:, k % 2, NF, :],
                                 dense[bass.ds(c * CS + (k + 2) * P, P), :]).then_inc(s_dense[k % 2], 16)
            for k in range(2):
                sp.wait_ge(s_turned[k], turned(CHUNKS - 1, k, BATCHES))
                n = (CHUNKS - 1) * TILES + k + 2
                sp.dma_start(rows[:, k, NF, :], dense[n * P:(n + 1) * P, :]).then_inc(s_dense[k], 16)
            sp.wait_ge(s_out, 16 * (CHUNKS + 1))

        @block.gpsimd
        def _(pool):
            pool.memset(ident[:], 0.0).then_inc(s_zero, 1)
            pool.wait_ge(s_zero, 1)
            pool.affine_select(out=ident[:], in_=ident[:], compare_op=ALU.not_equal, fill=1.0, base=0,
                               pattern=[[-1, P]], channel_multiplier=1).then_inc(s_ident, 1)
            with pool.Fori(0, CHUNKS) as c:
                for k in range(TILES):
                    pool.wait_ge(s_idx[k], (c + 1) * 16)
                    pool.wait_ge(s_turned[k % 2], turned(c, k, 0))
                    pool.sem_inc(s_tile_open, 1)
                    for f in range(NF):
                        pool.indirect_dma_start(
                            rows[:, k % 2, f, :], None, tables[f],
                            bass.IndirectOffsetOnAxis(ap=idx[:, k, f:f + 1], axis=0),
                        ).then_inc(s_gathered[k % 2], 16)

        @block.tensor
        def _(pe):
            def turn(c, k):
                pe.wait_ge(s_gathered[k % 2], (slot_tiles(c, k) + 1) * (16 * NF))
                pe.wait_ge(s_dense[k % 2], (slot_tiles(c, k) + 1) * 16)
                for i in range(BATCHES):
                    u = k * BATCHES + i
                    f0, n = batch(i)
                    pe.wait_ge(s_xt[u % 2], bank_batches(c, u, 0))
                    for j in range(n):
                        last = nc.tensor.transpose(turn_ps[:, u % 2, j, :], rows[:, k % 2, f0 + j, :], ident[:])
                    last.then_inc(s_turned[k % 2], 1)

            def products(c, k):
                for u in ((k + 1) * BATCHES - 2, (k + 1) * BATCHES - 1):
                    pe.wait_ge(s_xt[u % 2], bank_batches(c, u, 1))
                for i in range(ROUNDS):
                    r = k * ROUNDS + i
                    pe.wait_ge(s_gram_act[r % 2], half_rounds(c, r) + 1)
                    pe.wait_ge(s_gram_dve[r % 2], half_rounds(c, r) + 1)
                    for j in range(ROUND):
                        grp = i * ROUND + j
                        last = nc.tensor.matmul(gram_ps[:, r % 2, j, 0:Q * NV], xt_blocks(k, grp),
                                                xt_columns(k, grp), start=True, stop=True)
                    last.then_inc(s_gram[r % 2], 1)

            def free(c, u):
                pe.wait_ge(s_taken[u % 2], shared_uses(c, u) + 1)

            def pack(c):
                for r in (TILES * ROUNDS - 2, TILES * ROUNDS - 1):
                    pe.wait_ge(s_gram_act[r % 2], half_rounds(c, r) + 2)
                    pe.wait_ge(s_gram_dve[r % 2], half_rounds(c, r) + 2)
                for i in range(PACKS):
                    u = PACK0 + i
                    free(c, u)
                    for j in range(min(TURN, NF - i * TURN)):
                        last = nc.tensor.transpose(shared_ps[:, u % 2, j * P:(j + 1) * P],
                                                   gram[:, i * TURN + j, :, :].rearrange("p t g -> p (t g)"), ident[:])
                    last.then_inc(s_shared[u % 2], 1)

            def pairs_back(c):
                taken(pe, c, Z0 - 1)
                for t in range(KZ):
                    u = Z0 + t
                    free(c, u)
                    for q in range(Q):
                        last = nc.tensor.transpose(shared_ps[0:KP, u % 2, q * P:(q + 1) * P],
                                                   packed[:, q, t * KP:(t + 1) * KP], ident[:])
                    last.then_inc(s_shared[u % 2], 1)

            def layers(c):
                taken(pe, c, L10 - 1)
                for n in range(N1):
                    u = L10 + n
                    free(c, u)
                    for t in range(KZ):
                        nc.tensor.matmul(shared_ps[:, u % 2, :], w1z[:, t, n * P:(n + 1) * P], zt[:, t, :],
                                         start=(t == 0), stop=False)
                    nc.tensor.matmul(shared_ps[:, u % 2, :], w1d[:, n * P:(n + 1) * P], xt[:, :, :, NF],
                                     start=False, stop=True).then_inc(s_shared[u % 2], 1)
                taken(pe, c, L20 - 1)
                for n in range(N2):
                    u = L20 + n
                    free(c, u)
                    for t in range(N1):
                        last = nc.tensor.matmul(shared_ps[:, u % 2, :], w2s[:, t, n * P:(n + 1) * P], h1[:, t, :],
                                                start=(t == 0), stop=(t == N1 - 1))
                    last.then_inc(s_shared[u % 2], 1)
                taken(pe, c, L30 - 1)
                free(c, L30)
                for t in range(N2):
                    last = nc.tensor.matmul(shared_ps[0:1, L30 % 2, :], w3s[:, t:t + 1], h2[:, t, :],
                                            start=(t == 0), stop=(t == N2 - 1))
                last.then_inc(s_shared[L30 % 2], 1)

            for slot in range(2):
                pe.sem_inc(s_turned[slot], 1)
            pe.wait_ge(s_ident, 1)
            pe.wait_ge(s_pads, 2)
            pe.wait_ge(s_weights, 16 * 6)
            with pe.Fori(0, CHUNKS) as c:
                for k in range(TILES):
                    turn(c, k)
                    products(c, k)
                pack(c)
                pairs_back(c)
                layers(c)

        def take_batch(eng, copy, c, k, i):
            u = k * BATCHES + i
            f0, n = batch(i)
            eng.wait_ge(s_turned[k % 2], turned(c, k, i + 1))
            copy(xt[:, k, :, f0:f0 + n].rearrange("p s f -> p f s"), turn_ps[:, u % 2, 0:n, :]).then_inc(s_xt[u % 2], 1)

        def take_round(eng, copy, c, k, i, quads, done):
            r = k * ROUNDS + i
            eng.wait_ge(s_gram[r % 2], half_rounds(c, r) + 1)
            for q in quads:
                p0 = q * QUAD
                last = copy(gram[p0:p0 + NV, :, k, i * ROUND:(i + 1) * ROUND].rearrange("p g s -> p s g"),
                            gram_ps[p0:p0 + NV, r % 2, :, q * NV:q * NV + NF])
            last.then_inc(done[r % 2], 1)

        def shared_done(eng, c, u):
            eng.wait_ge(s_shared[u % 2], shared_uses(c, u) + 1)

        @block.scalar
        def _(act):
            act.sem_inc(s_xt[0], 1)
            for b in range(2):
                act.sem_inc(s_gram_act[b], 1)
                act.sem_inc(s_taken[b], 1)
            act.sem_inc(s_out, 16)
            act.wait_ge(s_weights, 16 * 6)
            with act.Fori(0, CHUNKS) as c:
                for k in range(TILES):
                    for i in range(BATCHES):
                        if (k * BATCHES + i) % 2 == 0:
                            take_batch(act, nc.scalar.copy, c, k, i)
                    for i in range(ROUNDS):
                        take_round(act, nc.scalar.copy, c, k, i, (0, 1), s_gram_act)
                for t in range(KZ):
                    u = Z0 + t
                    shared_done(act, c, u)
                    nc.scalar.copy(zt[:, t, :].rearrange("p (k g q) -> p k q g", k=TILES, q=Q),
                                   shared_ps[0:KP, u % 2, :].rearrange("p (q k g) -> p k q g", k=TILES, q=Q)
                                   ).then_inc(s_taken[u % 2], 1)
                for n in range(N1):
                    u = L10 + n
                    shared_done(act, c, u)
                    nc.scalar.activation(h1[:, n, :], shared_ps[:, u % 2, :], ACT.Relu,
                                         bias=b1s[:, n:n + 1]).then_inc(s_taken[u % 2], 1)
                for n in range(N2):
                    u = L20 + n
                    shared_done(act, c, u)
                    nc.scalar.activation(h2[:, n, :], shared_ps[:, u % 2, :], ACT.Relu,
                                         bias=b2s[:, n:n + 1]).then_inc(s_taken[u % 2], 1)
                shared_done(act, c, L30)
                act.wait_ge(s_out, (c + 1) * 16)
                nc.scalar.copy(y_row[:], shared_ps[0:1, L30 % 2, :]).then_inc(s_taken[L30 % 2], 1)
                act.wait_ge(s_taken[L30 % 2], shared_uses(c, L30) + 2)
                act.dma_start(y[bass.ds(c * CS, CS), :].rearrange("s o -> o s"), y_row[:]).then_inc(s_out, 16)

        @block.vector
        def _(dve):
            nc.vector.memset(xt[:, :, :, NV:QUAD], 0.0).then_inc(s_pads, 1)
            nc.vector.memset(gram[:], 0.0).then_inc(s_pads, 1)
            dve.sem_inc(s_xt[1], 1)
            for b in range(2):
                dve.sem_inc(s_gram_dve[b], 1)
            dve.wait_ge(s_pads, 2)
            with dve.Fori(0, CHUNKS) as c:
                for k in range(TILES):
                    for i in range(BATCHES):
                        if (k * BATCHES + i) % 2 == 1:
                            take_batch(dve, nc.vector.tensor_copy, c, k, i)
                    for i in range(ROUNDS):
                        take_round(dve, nc.vector.tensor_copy, c, k, i, (2, 3), s_gram_dve)
                for i in range(PACKS):
                    u = PACK0 + i
                    shared_done(dve, c, u)
                    for j in range(min(TURN, NF - i * TURN)):
                        g = i * TURN + j
                        turned = shared_ps[:, u % 2, j * P:(j + 1) * P].rearrange("p (q f) -> p q f", q=Q)
                        last = nc.vector.tensor_copy(packed[:, :, pair_start(g):pair_start(g) + NF - g],
                                                     turned[:, :, g + 1:NV])
                    last.then_inc(s_taken[u % 2], 1)


_INS = (["r_dense_x", "ids"] + [f"tbl_{f}" for f in range(NF)] + ["W_top1", "b_top1", "W_top2", "b_top2", "W_top3"])


def kernel(**inputs):
    import numpy as np
    import concourse.bacc as bacc
    from concourse.bass_utils import run_bass_kernel_spmd as run

    nc = bacc.Bacc("TRN2", target_bir_lowering=False, num_devices=1)
    arrays, a = {}, {}
    for name in _INS:
        x = np.ascontiguousarray(inputs[name])
        arrays[f"in_{name}"] = x
        a[name] = nc.dram_tensor(f"in_{name}", x.shape, mybir.dt.from_np(x.dtype), kind="ExternalInput").ap()
    y = nc.dram_tensor("out_y", (B, 1), F32, kind="ExternalOutput").ap()
    build(nc, a["r_dense_x"], a["ids"], [a[f"tbl_{f}"] for f in range(NF)], a["W_top1"], a["b_top1"],
          a["W_top2"], a["b_top2"], a["W_top3"], y)
    r = run(nc, [arrays], core_ids=[0])
    return r.results[0]["out_y"]
```

```python
from contextlib import ExitStack

import concourse.bass as bass
from concourse import mybir

F32 = mybir.dt.float32
F32R = mybir.dt.float32r
I32 = mybir.dt.int32
ALU = mybir.AluOpType
ACT = mybir.ActivationFunctionType

P = 128
NF = 26
NV = NF + 1
D = 128
B = 2048
TILES = 4
CS = TILES * P
CHUNKS = B // CS
QUAD = 32
Q = P // QUAD
GROUPS = P // Q
ROUND = 8
ROUNDS = GROUPS // ROUND
PAIRS = NV * (NV - 1) // 2
KZ = 3
KP = PAIRS // KZ
H1, H2 = 512, 256
N1, N2 = H1 // P, H2 // P
TURN = 4

LOOKED = {2: 8, 5: 8, 8: 8, 10: 8, 23: 8, 1: 10}
LF = list(LOOKED)
NL = len(LF)
LP = 125
HALF = 2
HS = HALF * P
PART = {f: LOOKED[f] // 2 for f in LF}
PARTS = max(PART.values())
TURNS = [(0, 3, 6, 9), (12, 15, 18, 21), (13, 16, 19, 22), (11, 14, 17, 20), (4, 7), (24, 25, 26)]
ROWS = [f for t in TURNS for f in t]
GATHERED = [f for f in ROWS if f < NF]
DENSE_SLOT = ROWS.index(NF)
NG = len(GATHERED)
BATCHES = len(TURNS)
PACKS = -(-NF // TURN)
Z0 = PACKS
L10 = Z0 + KZ
L20 = L10 + N1
L30 = L20 + N2
USES = L30 + 1
BANK_USES = [-(-USES // 2), USES // 2]

FIRST_STEPS = [
    "T0 E0 E1 L0 E2 T1 E3 L1 E4 T2 E5 L2 E6 T3 L3 E7 E8 T4 E9 L4 T5 G0 E10 L5 G1 G2 E11 G3".split(),
    "T0 E12 T1 L0 E13 T2 L1 T3 L2 T4 E14 L3 T5 E15 G0 L4 G1 E16 L5 G2 G3".split(),
]
LATER_STEPS = "T0 L0 T1 L1 T2 L2 T3 L3 T4 L4 T5 L5 G0 G1 G2 G3".split()
LAST_STEPS = "T0 T1 T2 T3 T4 T5 G0 G1 G2 G3".split()

assert KP * KZ == PAIRS and KP <= P and NV <= QUAD and D == P and LP * max(LOOKED.values()) == 1250
assert sorted(ROWS + LF) == list(range(NV)) and TILES == 2 * HALF


def runs(batch):
    out, at = [], 0
    while at < len(batch):
        n = 1
        while at + n < len(batch) and (n == 1 or batch[at + n] - batch[at + n - 1] == batch[at + 1] - batch[at]):
            n += 1
        if n == 2 and len(batch) - at > 2:
            n = 1
        out.append((at, batch[at], batch[at + 1] - batch[at] if n > 1 else 1, n))
        at += n
    return out


def in_first(c):
    return isinstance(c, int) and c == 0


def in_last(c):
    return isinstance(c, int) and c == CHUNKS - 1


def lookup_halves(c, k):
    if in_last(c) and k >= HALF:
        return []
    return [divmod(k * NL + j, 2) for j in range(NL)]


def tile_steps(c, k):
    halves = lookup_halves(c, k)
    for name in FIRST_STEPS[k] if k < HALF else LATER_STEPS if halves else LAST_STEPS:
        kind, n = name[0], int(name[1:])
        if kind == "L":
            yield kind, *halves[n]
        elif not (kind == "E" and in_first(c)):
            yield kind, n, 0


def pair_start(g):
    return g * NV - g * (g + 1) // 2


def build(nc, dense, ids, ids_t, tables, w1, b1, w2, b2, w3, y):
    with ExitStack() as ctx:
        def sb(name, shape, dt=F32):
            return ctx.enter_context(nc.sbuf_tensor(name, shape, dt))

        def psum(name, shape):
            return ctx.enter_context(nc.psum_tensor(name, shape, F32))

        def sem(name):
            return ctx.enter_context(nc.semaphore(name))

        idx = sb("idx", [P, TILES, NF], I32)
        rows = sb("rows", [P, 2, len(ROWS), D])
        xt = sb("xt", [P, TILES, P, QUAD])
        gram = sb("gram", [P, NF, TILES, GROUPS])
        packed = sb("packed", [P, Q, PAIRS])
        zt = sb("zt", [KP, KZ, CS])
        xd = sb("xd", [P, CS])
        h1 = sb("h1", [P, N1, CS])
        h2 = packed[:, :, :].rearrange("p q z -> p (q z)")[:, 0:N2 * CS].rearrange("p (n s) -> p n s", n=N2)
        y_row = sb("y_row", [1, CS])
        w1z = sb("w1z", [KP, KZ, H1])
        w1d = sb("w1d", [P, H1])
        w2s = sb("w2s", [P, N1, H2])
        w3s = sb("w3s", [P, N2])
        b1s = sb("b1s", [P, N1])
        b2s = sb("b2s", [P, N2])
        ident = sb("ident", [P, P])
        table_at = {f: sum(LOOKED[g] for g in LF[:i]) for i, f in enumerate(LF)}
        table_hi = sb("table_hi", [LP, sum(LOOKED.values()), D], F32R)
        table_lo = sb("table_lo", [LP, sum(LOOKED.values()), D], F32R)
        masks = sb("masks", [LP, 2, PARTS, HS], F32R)
        ids_b = sb("ids_b", [LP, 2, HS], I32)
        row_int = sb("row_int", [LP, 2, PARTS * 2], I32)
        row_no = sb("row_no", [LP, 2, PARTS * 2])
        arrive = xt[0:LP, HALF:TILES, :, :].rearrange("p t s f -> p (t s f)")
        row_kind = {n: i for i, n in enumerate(sorted(set(LOOKED.values())))}

        turn_ps = psum("turn_ps", [P, TURN * P])
        look_ps = psum("look_ps", [P, CS])
        gram_ps = psum("gram_ps", [P, 2, ROUND, P])
        shared_ps = psum("shared_ps", [P, 2, CS])

        s_idx = [sem(f"s_idx{k}") for k in range(TILES)]
        s_gathered = [sem(f"s_gathered{s}") for s in range(2)]
        s_tile_open = sem("s_tile_open")
        s_dense = [sem(f"s_dense{s}") for s in range(2)]
        s_weights = sem("s_weights")
        s_table = [sem(f"s_table{i}") for i in range(NL)]
        s_table_hi = sem("s_table_hi")
        s_table_lo = sem("s_table_lo")
        s_row_int = sem("s_row_int")
        s_row_no = sem("s_row_no")
        s_ids = [sem(f"s_ids{i}") for i in range(2)]
        s_mask = [sem(f"s_mask{e}") for e in range(2)]
        s_mask_used = sem("s_mask_used")
        s_zero = sem("s_zero")
        s_ident = sem("s_ident")
        s_pads = sem("s_pads")
        s_turned = [sem(f"s_turned{s}") for s in range(2)]
        s_xt = sem("s_xt")
        s_xd = sem("s_xd")
        s_look = sem("s_look")
        s_look_taken = sem("s_look_taken")
        s_gram = [sem(f"s_gram{b}") for b in range(2)]
        s_gram_act = [sem(f"s_gram_act{b}") for b in range(2)]
        s_gram_dve = [sem(f"s_gram_dve{b}") for b in range(2)]
        s_shared = [sem(f"s_shared{b}") for b in range(2)]
        s_taken = [sem(f"s_taken{b}") for b in range(2)]
        s_y = sem("s_y")
        s_out = sem("s_out")

        def xt_columns(k, grp):
            return xt[:, k, grp * Q:(grp + 1) * Q, 0:NF]

        def xt_blocks(k, grp):
            return xt[:, k, grp * Q:(grp + 1) * Q, :].rearrange("p q f -> p (q f)")

        def slot_tiles(c, k):
            return c * (TILES // 2) + k // 2

        def turned(c, k, n):
            return slot_tiles(c, k) * BATCHES + (n + 1)

        def turn_bank(c, k, i):
            return look_ps if in_last(c) and k >= HALF and i % 2 else turn_ps

        def batches(c, k, n):
            return c * (TILES * BATCHES) + (k * BATCHES + n + 1)

        def half_rounds(c, r):
            return c * (TILES * ROUNDS // 2) + r // 2

        def shared_uses(c, u):
            return c * BANK_USES[u % 2] + u // 2

        def lookups(c, v):
            return c * (2 * NL) + (NL + v) if v >= 0 else v + NL

        def ids_value(c, v):
            return (c * NL + ((NL + v) // 2 + 1)) * 16

        def taken(eng, c, u):
            for v in (u - 1, u):
                eng.wait_ge(s_taken[v % 2], shared_uses(c, v) + 2)

        def after(v, e, n):
            return divmod(2 * v + e + n, 2)

        block = ctx.enter_context(nc.Block())

        def load_ids(sp, c, v):
            f = LF[v % NL]
            at = c * CS + (v // NL + 1) * HS
            slot = (v + NL) % 2
            sp.dma_start(ids_b[:, slot, :], ids_t[f:f + 1, bass.ds(at, HS)].to_broadcast([LP, HS])).then_inc(s_ids[slot], 16)

        def next_ids(sp, c, v):
            sp.wait_ge(s_mask[1], lookups(c, v) - 1)
            load_ids(sp, c, v)

        @block.sync
        def _(sp):
            for k in range(TILES):
                sp.dma_start(idx[:, k, :], ids[k * P:(k + 1) * P, :]).then_inc(s_idx[k], 16)
            for v in range(2):
                load_ids(sp, 0, v - NL)
            for s in range(2):
                sp.dma_start(rows[:, s, DENSE_SLOT, :], dense[s * P:(s + 1) * P, :]).then_inc(s_dense[s], 16)
            for i, f in enumerate(LF):
                n = LOOKED[f] * D
                at = table_at[f] * D
                for p0, p1 in ((0, 112), (112, LP)):
                    sp.dma_start(arrive[p0:p1, at:at + n],
                                 tables[f].rearrange("(p k) d -> p (k d)", p=LP)[p0:p1, :]).then_inc(s_table[i], 16)
            for v in range(2 - NL, 2):
                next_ids(sp, 0, v)

            def chunk(c):
                for k in range(TILES):
                    if not in_last(c):
                        sp.wait_ge(s_gathered[k % 2], (slot_tiles(c, k) + 1) * (16 * NG))
                        sp.dma_start(idx[:, k, :], ids[bass.ds((c + 1) * CS + k * P, P), :]).then_inc(s_idx[k], 16)
                    for v, e in lookup_halves(c, k):
                        if e == 0 and not (in_last(c) and v + 2 >= NL):
                            next_ids(sp, c, v + 2)
                    if not (in_last(c) and k >= 2):
                        sp.wait_ge(s_turned[k % 2], turned(c, k, BATCHES))
                        sp.dma_start(rows[:, k % 2, DENSE_SLOT, :],
                                     dense[bass.ds(c * CS + (k + 2) * P, P), :]).then_inc(s_dense[k % 2], 16)

            with sp.Fori(0, CHUNKS - 1) as c:
                chunk(c)
            chunk(CHUNKS - 1)
            sp.wait_ge(s_out, 16 * (CHUNKS + 1))

        @block.gpsimd
        def _(pool):
            pool.memset(ident[:], 0.0).then_inc(s_zero, 1)
            pool.wait_ge(s_zero, 1)
            pool.affine_select(out=ident[:], in_=ident[:], compare_op=ALU.not_equal, fill=1.0, base=0,
                               pattern=[[-1, P]], channel_multiplier=1).then_inc(s_ident, 1)
            for n, i in row_kind.items():
                last = pool.iota(row_int[:, i, 0:n], pattern=[[1, n]], base=0, channel_multiplier=n)
            last.then_inc(s_row_int, 1)
            with pool.Fori(0, CHUNKS) as c:
                for k in range(TILES):
                    pool.wait_ge(s_idx[k], (c + 1) * 16)
                    pool.wait_ge(s_turned[k % 2], turned(c, k, 0))
                    pool.sem_inc(s_tile_open, 1)
                    for slot, f in enumerate(ROWS):
                        if f == NF:
                            continue
                        pool.indirect_dma_start(
                            rows[:, k % 2, slot, :], None, tables[f],
                            bass.IndirectOffsetOnAxis(ap=idx[:, k, f:f + 1], axis=0),
                        ).then_inc(s_gathered[k % 2], 16)

        @block.tensor
        def _(pe):
            def turn(c, k, i):
                if i == 0:
                    pe.wait_ge(s_gathered[k % 2], (slot_tiles(c, k) + 1) * (16 * NG))
                    pe.wait_ge(s_dense[k % 2], (slot_tiles(c, k) + 1) * 16)
                if i == BATCHES - 1 and k == 0 and not in_first(c):
                    pe.wait_ge(s_xd, c)
                two = in_last(c) and k >= HALF and i > 0
                if two:
                    pe.wait_ge(s_look_taken, lookups(c, NL) + 1)
                pe.wait_ge(s_xt, batches(c, k, i - 1 if two else i))
                for j, f in enumerate(TURNS[i]):
                    last = nc.tensor.transpose(turn_bank(c, k, i)[:, j * P:(j + 1) * P],
                                               rows[:, k % 2, ROWS.index(f), :], ident[:])
                last.then_inc(s_turned[k % 2], 1)

            def look_up(c, v, e):
                f = LF[v % NL]
                if e == 0:
                    pe.wait_ge(s_look_taken, lookups(c, v) + 1)
                pe.wait_ge(s_mask[e], lookups(c, v) + 1)
                for k in range(PART[f]):
                    for table in (table_hi, table_lo):
                        first = e == 0 and k == 0 and table is table_hi
                        stop = e == 1 and k == PART[f] - 1 and table is table_lo
                        last = nc.tensor.matmul(look_ps[:, 0:HS],
                                                table[:, table_at[f] + e * PART[f] + k, :], masks[:, e, k, :],
                                                start=first, stop=stop)
                last.then_inc(s_look if e else s_mask_used, 1)

            def products(c, k, i):
                if i == 0:
                    pe.wait_ge(s_xt, batches(c, k, BATCHES))
                    if k % HALF == 0:
                        pe.wait_ge(s_look_taken, lookups(c, k // HALF * NL) + 1)
                r = k * ROUNDS + i
                pe.wait_ge(s_gram_act[r % 2], half_rounds(c, r) + 1)
                pe.wait_ge(s_gram_dve[r % 2], half_rounds(c, r) + 1)
                for j in range(ROUND):
                    grp = i * ROUND + j
                    last = nc.tensor.matmul(gram_ps[:, r % 2, j, 0:Q * NF], xt_blocks(k, grp),
                                            xt_columns(k, grp), start=True, stop=True)
                last.then_inc(s_gram[r % 2], 1)

            def free(c, u):
                pe.wait_ge(s_taken[u % 2], shared_uses(c, u) + 1)

            def pack(c, i):
                if i == 0:
                    for r in (TILES * ROUNDS - 2, TILES * ROUNDS - 1):
                        pe.wait_ge(s_gram_act[r % 2], half_rounds(c, r) + 2)
                        pe.wait_ge(s_gram_dve[r % 2], half_rounds(c, r) + 2)
                free(c, i)
                for j in range(min(TURN, NF - i * TURN)):
                    last = nc.tensor.transpose(shared_ps[:, i % 2, j * P:(j + 1) * P],
                                               gram[:, i * TURN + j, :, :].rearrange("p t g -> p (t g)"), ident[:])
                return last

            def pairs_back(c, t):
                if t == 0:
                    taken(pe, c, Z0 - 1)
                u = Z0 + t
                free(c, u)
                for q in range(Q):
                    last = nc.tensor.transpose(shared_ps[0:KP, u % 2, q * P:(q + 1) * P],
                                               packed[:, q, t * KP:(t + 1) * KP], ident[:])
                return last

            def layer1(c, n):
                if n == 0:
                    taken(pe, c, L10 - 1)
                    pe.wait_ge(s_xd, c + 1)
                u = L10 + n
                free(c, u)
                nc.tensor.matmul(shared_ps[:, u % 2, :], w1d[:, n * P:(n + 1) * P], xd[:], start=True, stop=False)
                for t in range(KZ):
                    last = nc.tensor.matmul(shared_ps[:, u % 2, :], w1z[:, t, n * P:(n + 1) * P], zt[:, t, :],
                                            start=False, stop=(t == KZ - 1))
                return last

            def layer2(c, n):
                if n == 0:
                    taken(pe, c, L20 - 1)
                u = L20 + n
                free(c, u)
                for t in range(N1):
                    last = nc.tensor.matmul(shared_ps[:, u % 2, :], w2s[:, t, n * P:(n + 1) * P], h1[:, t, :],
                                            start=(t == 0), stop=(t == N1 - 1))
                return last

            def layer3(c):
                taken(pe, c, L30 - 1)
                free(c, L30)
                for t in range(N2):
                    last = nc.tensor.matmul(shared_ps[0:1, L30 % 2, :], w3s[:, t:t + 1], h2[:, t, :],
                                            start=(t == 0), stop=(t == N2 - 1))
                return last

            def end_step(c, u):
                if u < Z0:
                    last = pack(c, u)
                elif u < L10:
                    last = pairs_back(c, u - Z0)
                elif u < L20:
                    last = layer1(c, u - L10)
                elif u < L30:
                    last = layer2(c, u - L20)
                else:
                    last = layer3(c)
                last.then_inc(s_shared[u % 2], 1)

            for slot in range(2):
                pe.sem_inc(s_turned[slot], 1)
            pe.wait_ge(s_ident, 1)
            for v in range(-NL, 0):
                pe.wait_ge(s_table_lo, v + NL + 1)
                for e in range(2):
                    look_up(0, v, e)
            pe.wait_ge(s_pads, 2)
            pe.wait_ge(s_weights, 16 * 6)

            def chunk(c):
                for k in range(TILES):
                    for kind, n, e in tile_steps(c, k):
                        if kind == "T":
                            turn(c, k, n)
                        elif kind == "L":
                            look_up(c, n, e)
                        elif kind == "G":
                            products(c, k, n)
                        else:
                            end_step(c - 1, n)

            chunk(0)
            with pe.Fori(1, CHUNKS - 1) as c:
                chunk(c)
            chunk(CHUNKS - 1)
            for u in range(USES):
                end_step(CHUNKS - 1, u)

        def take_batch(eng, copy, c, k, i):
            eng.wait_ge(s_turned[k % 2], turned(c, k, i + 1))
            for at, f, step, n in runs(TURNS[i]):
                last = copy(xt[:, k, :, f:f + (n - 1) * step + 1:step].rearrange("p s f -> p f s"),
                            turn_bank(c, k, i)[:, at * P:(at + n) * P].rearrange("p (f s) -> p f s", f=n))
            last.then_inc(s_xt, 1)

        def take_round(eng, copy, c, k, i, quads, done):
            r = k * ROUNDS + i
            eng.wait_ge(s_gram[r % 2], half_rounds(c, r) + 1)
            for q in quads:
                p0 = q * QUAD
                last = copy(gram[p0:p0 + NV, :, k, i * ROUND:(i + 1) * ROUND].rearrange("p g s -> p s g"),
                            gram_ps[p0:p0 + NV, r % 2, :, q * NF:(q + 1) * NF])
            last.then_inc(done[r % 2], 1)

        def take_pack(eng, copy, c, i):
            shared_done(eng, c, i)
            for j in range(min(TURN, NF - i * TURN)):
                g = i * TURN + j
                columns = shared_ps[:, i % 2, j * P:(j + 1) * P].rearrange("p (q f) -> p q f", q=Q)
                last = copy(packed[:, :, pair_start(g):pair_start(g) + NF - g], columns[:, :, g + 1:NV])
            last.then_inc(s_taken[i % 2], 1)

        def shared_done(eng, c, u):
            eng.wait_ge(s_shared[u % 2], shared_uses(c, u) + 1)

        @block.scalar
        def _(act):
            act.dma_start(w1z[:], w1[0:PAIRS, :].rearrange("(c p) n -> p c n", p=KP)).then_inc(s_weights, 16)
            act.dma_start(w1d[:], w1[PAIRS:PAIRS + D, :]).then_inc(s_weights, 16)
            act.dma_start(w2s[:], w2.rearrange("(c p) n -> p c n", p=P)).then_inc(s_weights, 16)
            with nc.allow_non_contiguous_dma(reason="small vectors, one value per partition"):
                act.dma_start(w3s[:], w3.rearrange("(c p) o -> p (c o)", p=P)).then_inc(s_weights, 16)
                act.dma_start(b1s[:], b1.rearrange("(c p) -> p c", p=P)).then_inc(s_weights, 16)
                act.dma_start(b2s[:], b2.rearrange("(c p) -> p c", p=P)).then_inc(s_weights, 16)
            act.sem_inc(s_xt, 1)
            act.sem_inc(s_look_taken, 1)
            for b in range(2):
                act.sem_inc(s_gram_act[b], 1)
                act.sem_inc(s_taken[b], 1)
            act.sem_inc(s_out, 16)
            def take_lookup(c, v):
                k = 0 if v < 0 or v >= NL else HALF
                act.wait_ge(s_look, lookups(c, v) + 1)
                nc.scalar.copy(xt[:, k:k + HALF, :, LF[v % NL]],
                               look_ps[:, 0:HS].rearrange("p (k s) -> p k s", k=HALF)).then_inc(s_look_taken, 1)

            for i, f in enumerate(LF):
                at, n = table_at[f], LOOKED[f]
                act.wait_ge(s_table[i], 32)
                nc.scalar.copy(table_hi[:, at:at + n, :].rearrange("p k d -> p (k d)"),
                               arrive[:, at * D:(at + n) * D]).then_inc(s_table_hi, 1)
                if i >= 1:
                    take_lookup(0, i - 1 - NL)
            take_lookup(0, -1)
            act.wait_ge(s_weights, 16 * 6)

            def end_step(c, u):
                b = u % 2
                if u >= Z0:
                    shared_done(act, c, u)
                if u < Z0:
                    if b == 1:
                        take_pack(act, nc.scalar.copy, c, u)
                    return
                if u < L10:
                    last = nc.scalar.copy(zt[:, u - Z0, :].rearrange("p (k g q) -> p k q g", k=TILES, q=Q),
                                          shared_ps[0:KP, b, :].rearrange("p (q k g) -> p k q g", k=TILES, q=Q))
                elif u < L20:
                    n = u - L10
                    last = nc.scalar.activation(h1[:, n, :], shared_ps[:, b, :], ACT.Relu, bias=b1s[:, n:n + 1])
                elif u < L30:
                    n = u - L20
                    last = nc.scalar.activation(h2[:, n, :], shared_ps[:, b, :], ACT.Relu, bias=b2s[:, n:n + 1])
                else:
                    act.wait_ge(s_out, (c + 1) * 16)
                    last = nc.scalar.copy(y_row[:], shared_ps[0:1, b, :])
                last.then_inc(s_taken[b], 1)
                if u == L30:
                    act.wait_ge(s_taken[b], shared_uses(c, u) + 2)
                    act.dma_start(y[bass.ds(c * CS, CS), :].rearrange("s o -> o s"), y_row[:]).then_inc(s_out, 16)

            def chunk(c):
                for k in range(TILES):
                    for kind, n, e in tile_steps(c, k):
                        if kind == "T":
                            take_batch(act, nc.scalar.copy, c, k, n)
                        elif kind == "L" and e == 1:
                            take_lookup(c, n)
                        elif kind == "G":
                            take_round(act, nc.scalar.copy, c, k, n, (0, 1, 2), s_gram_act)
                        elif kind == "E":
                            end_step(c - 1, n)

            chunk(0)
            with act.Fori(1, CHUNKS - 1) as c:
                chunk(c)
            chunk(CHUNKS - 1)
            for u in range(USES):
                end_step(CHUNKS - 1, u)

        @block.vector
        def _(dve):
            nc.vector.memset(gram[:], 0.0).then_inc(s_pads, 1)
            for b in range(2):
                dve.sem_inc(s_gram_dve[b], 1)
            dve.wait_ge(s_row_int, 1)
            for n, i in row_kind.items():
                last = nc.vector.tensor_copy(row_no[:, i, 0:n], row_int[:, i, 0:n])
            last.then_inc(s_row_no, 1)
            dve.wait_ge(s_pads, 1)
            dve.wait_ge(s_row_no, 1)

            def mask(c, v, e):
                f = LF[v % NL]
                slot = (v + NL) % 2
                if e == 0:
                    dve.wait_ge(s_ids[slot], ids_value(c, v))
                if v > -NL:
                    if e == 0:
                        dve.wait_ge(s_mask_used, lookups(c, v))
                    else:
                        dve.wait_ge(s_look, lookups(c, v))
                for k in range(PART[f]):
                    at = e * PART[f] + k
                    last = nc.vector.tensor_scalar(masks[:, e, k, :], ids_b[:, slot, :],
                                                   row_no[:, row_kind[LOOKED[f]], at:at + 1], None, ALU.is_equal)
                last.then_inc(s_mask[e], 1)

            for i, f in enumerate(LF):
                at, n = table_at[f], LOOKED[f]
                dve.wait_ge(s_table[i], 32)
                dve.wait_ge(s_table_hi, i + 1)
                nc.vector.tensor_tensor(table_lo[:, at:at + n, :].rearrange("p k d -> p (k d)"),
                                        arrive[:, at * D:(at + n) * D],
                                        table_hi[:, at:at + n, :].rearrange("p k d -> p (k d)").bitcast(F32),
                                        ALU.subtract).then_inc(s_table_lo, 1)
                for e in range(2):
                    mask(0, i - NL, e)
            dve.wait_ge(s_table_lo, NL)
            nc.vector.memset(xt[:, :, :, NV:QUAD], 0.0).then_inc(s_pads, 1)
            for e in range(2):
                mask(0, 0, e)

            def end_step(c, u):
                if u < Z0 and u % 2 == 0:
                    take_pack(dve, nc.vector.tensor_copy, c, u)

            def chunk(c):
                for k in range(TILES):
                    for kind, n, e in tile_steps(c, k):
                        if kind == "L":
                            v1, e1 = after(n, e, 2)
                            if not (in_last(c) and v1 >= NL):
                                mask(c, v1, e1)
                        elif kind == "G":
                            take_round(dve, nc.vector.tensor_copy, c, k, n, (3,), s_gram_dve)
                        elif kind == "E":
                            end_step(c - 1, n)
                dve.wait_ge(s_xt, batches(c, TILES - 1, BATCHES))
                nc.vector.tensor_copy(xd[:].rearrange("p (k s) -> p k s", k=TILES), xt[:, :, :, NF]).then_inc(s_xd, 1)

            chunk(0)
            with dve.Fori(1, CHUNKS - 1) as c:
                chunk(c)
            chunk(CHUNKS - 1)
            for u in range(USES):
                end_step(CHUNKS - 1, u)


_INS = (["r_dense_x", "ids"] + [f"tbl_{f}" for f in range(NF)] + ["W_top1", "b_top1", "W_top2", "b_top2", "W_top3"])


def kernel(**inputs):
    import numpy as np
    import concourse.bacc as bacc
    from concourse.bass_utils import run_bass_kernel_spmd as run

    nc = bacc.Bacc("TRN2", target_bir_lowering=False, num_devices=1)
    arrays, a = {}, {}
    for name in _INS:
        x = np.ascontiguousarray(inputs[name])
        arrays[f"in_{name}"] = x
        a[name] = nc.dram_tensor(f"in_{name}", x.shape, mybir.dt.from_np(x.dtype), kind="ExternalInput").ap()
    arrays["in_ids_t"] = np.ascontiguousarray(inputs["ids"].T)
    ids_t = nc.dram_tensor("in_ids_t", (NF, B), mybir.dt.from_np(arrays["in_ids_t"].dtype), kind="ExternalInput").ap()
    y = nc.dram_tensor("out_y", (B, 1), F32, kind="ExternalOutput").ap()
    build(nc, a["r_dense_x"], a["ids"], ids_t, [a[f"tbl_{f}"] for f in range(NF)], a["W_top1"], a["b_top1"],
          a["W_top2"], a["b_top2"], a["W_top3"], y)
    r = run(nc, [arrays], core_ids=[0])
    return r.results[0]["out_y"]
```

```python
from contextlib import ExitStack

import concourse.bass as bass
from concourse import mybir

F32 = mybir.dt.float32
F32R = mybir.dt.float32r
I32 = mybir.dt.int32
ALU = mybir.AluOpType
ACT = mybir.ActivationFunctionType

P = 128
NF = 26
NV = NF + 1
D = 128
B = 2048
TILES = 4
CS = TILES * P
CHUNKS = B // CS
HALF = TILES // 2
HS = HALF * P
QUAD = 32
Q = P // QUAD
GROUPS = P // Q
ROUND = 8
ROUNDS = GROUPS // ROUND
GG = NF // 2
PAIRS = NV * (NV - 1) // 2
KZ = 3
K1 = KZ + 1
H1, H2 = 512, 256
N1, N2 = H1 // P, H2 // P
TURN = 4

LOOKED = {2: 8, 5: 8, 8: 8, 10: 8, 23: 8, 1: 10}
LF = list(LOOKED)
NL = len(LF)
LP = 125
PART = {f: LOOKED[f] // 2 for f in LF}
PARTS = max(PART.values())
TURNS = [(0, 3, 6, 9), (12, 15, 18, 21), (13, 16, 19, 22), (11, 14, 17, 20), (4, 7, 24, 25)]
ROWS = [f for t in TURNS for f in t]
NG = len(ROWS)
BATCHES = len(TURNS)

COPIED = list(range(NF, NF - KZ * Q, -1))
COPY_STEPS = 3
BY_DMA = list(range(NF - KZ * Q, 0, -1))
LAST_POOL = BY_DMA[::3]
LAST_SP = [j for j in BY_DMA if j not in LAST_POOL]
IDS = 3
PAIRS_STEP = 3
L20 = N1
L30 = L20 + N2
USES = L30 + 1
SPLITS = K1 + N1

L_FIRST = 8
STEPS = [
    "T0 L0 C0 T1 L1 C1 T2 L2 C2 T3 L3 T4 L4 S3 L5 G0 L6 G1 L7 G2 G3".split(),
    "T0 L0 T1 L1 T2 L2 T3 T4 L3 S0 S1 S2 G0 G1 E0 E1 E2 E3 G2 E4 E5 G3 E6".split(),
]
LAST_STEPS = [
    "T0 T1 T2 T3 T4 C0 G0 C1 G1 C2 G2 S3 G3".split(),
    "T0 S0 S1 S2 T1 E0 T2 E1 T3 E2 E3 T4 G0 G1 G2 G3".split(),
]
FINAL_STEPS = "C0 C1 C2 F4 F5 F6 S3 S0 S1 S2 E0 E1 E2 E3 E4 E5 E6".split()
FIRST_STEPS = "L0 L1 L2 L3 L4 L5 L6 L7 T0 L8 T1 L9 T2 L10 T3 L11 T4".split()

assert 2 * NL % IDS == 0 and len(FIRST_STEPS) == 2 * NL + BATCHES
assert N2 == 2 and NV <= QUAD and D == P and LP * max(LOOKED.values()) == 1250
assert sorted(ROWS + LF) == list(range(NF)) and TILES == 4 and USES == 7 and 2 * PARTS == 10


def places():
    place = {j: (i // Q, i % Q * QUAD) for i, j in enumerate(COPIED)}
    room = {j: QUAD - j for j in COPIED}
    for j in BY_DMA:
        best = min((j0 for j0 in room if room[j0] >= j), key=lambda j0: room[j0])
        t, z = place[best]
        place[j] = (t, z + QUAD - room[best])
        room[best] -= j
    return place


PLACE = places()


def runs(batch):
    out, at = [], 0
    while at < len(batch):
        n = 1
        while at + n < len(batch) and (n == 1 or batch[at + n] - batch[at + n - 1] == batch[at + 1] - batch[at]):
            n += 1
        out.append((at, batch[at], batch[at + 1] - batch[at] if n > 1 else 1, n))
        at += n
    return out


def in_first(c):
    return isinstance(c, int) and c == 0


def in_last(c):
    return isinstance(c, int) and c == CHUNKS - 1


def in_last_tile(c, k):
    return in_last(c) and k == TILES - 1


def lookup_halves(c, k):
    if in_last(c) and k >= HALF:
        return []
    start = k // HALF * 2 * NL + (L_FIRST if k % HALF else 0)
    return [divmod(start + j, 2) for j in range(2 * NL - L_FIRST if k % HALF else L_FIRST)]


def tile_steps(c, k):
    halves = lookup_halves(c, k)
    for name in (LAST_STEPS if in_last(c) and k >= HALF else STEPS)[k % HALF]:
        kind, n = name[0], int(name[1:])
        if kind == "L":
            if halves:
                yield kind, *halves[n]
        elif in_first(c) and (kind in "CSE" and k < HALF or kind == "T" and k == 0):
            continue
        else:
            yield kind, n, 0


def first_steps():
    for name in FIRST_STEPS:
        yield name[0], int(name[1:])


def final_steps():
    for name in FINAL_STEPS:
        yield name[0].replace("F", "E"), int(name[1:]), 0 if name[0] == "F" else 1


def half_before(c, k):
    return (c, 0) if k >= HALF else (c - 1, 1)


def build(nc, dense_t, ids, ids_t, tables, w1z, w1, b1, w2, b2, w3, y):
    with ExitStack() as ctx:
        def sb(name, shape, dt=F32):
            return ctx.enter_context(nc.sbuf_tensor(name, shape, dt))

        def psum(name, shape):
            return ctx.enter_context(nc.psum_tensor(name, shape, F32))

        def sem(name):
            return ctx.enter_context(nc.semaphore(name))

        idx = sb("idx", [P, TILES, NF], I32)
        rows = sb("rows", [P, 2, NG, D])
        xt = sb("xt", [P, TILES, P, QUAD])
        gram = sb("gram", [P, GG, HS])
        pairs = sb("pairs", [P, KZ, HS])
        whole = sb("whole", [P, 2, HS])
        h2 = whole
        z_hi = sb("z_hi", [P, K1, HS], F32R)
        z_lo = sb("z_lo", [P, K1, HS], F32R)
        h_hi = sb("h_hi", [P, N1, HS], F32R)
        h_lo = sb("h_lo", [P, N1, HS], F32R)
        y_row = whole[0:1, 1, :]
        dense_x = sb("dense_x", [P, HS])
        w1_hi = sb("w1_hi", [P, K1, H1], F32R)
        w1_lo = sb("w1_lo", [P, K1, H1], F32R)
        w2_hi = sb("w2_hi", [P, N1, H2], F32R)
        w2_lo = sb("w2_lo", [P, N1, H2], F32R)
        w3s = sb("w3s", [P, N2])
        b1s = sb("b1s", [P, N1])
        b2s = sb("b2s", [P, N2])
        ident = sb("ident", [P, P])
        table_at = {f: sum(LOOKED[g] for g in LF[:i]) for i, f in enumerate(LF)}
        table_hi = sb("table_hi", [LP, sum(LOOKED.values()), D], F32R)
        table_lo = sb("table_lo", [LP, sum(LOOKED.values()), D], F32R)
        masks = sb("masks", [LP, 2, PARTS, HS], F32R)
        ids_b = sb("ids_b", [LP, IDS, HS], I32)
        row_kind = {n: i for i, n in enumerate(sorted(set(LOOKED.values())))}
        row_int = sb("row_int", [LP, 2, PARTS * 2], I32)
        row_no = sb("row_no", [LP, 2, PARTS * 2])
        tables_in = xt[0:LP, HALF:TILES, :, :].rearrange("p t s f -> p (t s f)")
        weights_in = gram[:, :, :].rearrange("p g s -> p (g s)")
        w1z_in = weights_in[:, 0:KZ * H1].rearrange("p (c n) -> p c n", c=KZ)
        w1d_in = weights_in[:, KZ * H1:K1 * H1]
        w2_in = weights_in[:, K1 * H1:K1 * H1 + N1 * H2]

        turn_ps = psum("turn_ps", [P, TURN * P])
        look_ps = psum("look_ps", [P, TURN * P])
        gram_ps = psum("gram_ps", [P, 2, ROUND, P])
        shared_ps = psum("shared_ps", [P, 2, 2 * HS])

        s_idx = [sem(f"s_idx{k}") for k in range(TILES)]
        s_gathered = [sem(f"s_gathered{s}") for s in range(2)]
        s_last_rows = [sem(f"s_last_rows{i}") for i in range(BATCHES)]
        s_tile_open = sem("s_tile_open")
        s_load_open = sem("s_load_open")
        s_dense = sem("s_dense")
        s_dense_used = sem("s_dense_used")
        s_weights = sem("s_weights")
        s_w_hi = sem("s_w_hi")
        s_w_lo = sem("s_w_lo")
        s_table = [sem(f"s_table{i}") for i in range(NL)]
        s_table_hi = sem("s_table_hi")
        s_table_lo = sem("s_table_lo")
        s_row_int = sem("s_row_int")
        s_row_no = sem("s_row_no")
        s_ids = [sem(f"s_ids{i}") for i in range(IDS)]
        s_mask = [sem(f"s_mask{e}") for e in range(2)]
        s_mask_used = sem("s_mask_used")
        s_zero = sem("s_zero")
        s_ident = sem("s_ident")
        s_pads = sem("s_pads")
        s_no_pairs = sem("s_no_pairs")
        s_turned = [sem(f"s_turned{s}") for s in range(2)]
        s_xt = sem("s_xt")
        s_look = sem("s_look")
        s_look_taken = sem("s_look_taken")
        s_gram = [sem(f"s_gram{b}") for b in range(2)]
        s_gram_act = [sem(f"s_gram_act{b}") for b in range(2)]
        s_gram_dve = [sem(f"s_gram_dve{b}") for b in range(2)]
        s_shared = [sem(f"s_shared{b}") for b in range(2)]
        s_taken = [sem(f"s_taken{b}") for b in range(2)]
        s_pairs = [sem(f"s_pairs{b}") for b in range(2)]
        s_copied = {name: sem(f"s_copied_{name}") for name in ("act", "dve")}
        s_pairs_pool = sem("s_pairs_pool")
        s_pairs_upper = sem("s_pairs_upper")
        s_upper = sem("s_upper")
        s_split = sem("s_split")
        s_out = sem("s_out")

        def table_arrives(f):
            return tables_in[:, table_at[f] * D:(table_at[f] + LOOKED[f]) * D]

        def slot_tiles(c, k):
            return c * (TILES // 2) + k // 2

        def turned(c, k, n):
            return slot_tiles(c, k) * BATCHES + (n + 1)

        def batches(c, k, n):
            return c * (TILES * BATCHES) + (k * BATCHES + n + 1)

        def half_rounds(c, r):
            return c * (TILES * ROUNDS // 2) + r // 2

        def bank(h, u):
            return (h * USES + u) % 2

        def shared_uses(c, h, u):
            return c * USES + (h * USES + u) // 2

        def shared_done(eng, c, h, u):
            eng.wait_ge(s_shared[bank(h, u)], shared_uses(c, h, u) + 1)

        def taken(eng, c, h, u):
            for v in (u - 1, u):
                eng.wait_ge(s_taken[bank(h, v)], shared_uses(c, h, v) + 2)

        def splits(c, h, n):
            return c * (2 * SPLITS) + (h * SPLITS + n)

        def lookups(c, v):
            return c * (2 * NL) + (NL + v)

        def ids_value(c, v):
            return (c * (2 * NL // IDS) + ((NL + v) // IDS + 1)) * 16

        def turn_bank(c, k, i):
            return look_ps if in_last(c) and k >= HALF and i % 2 else turn_ps

        def load_ids(eng, c, v):
            f = LF[v % NL]
            at = c * CS + (v // NL + 1) * HS
            slot = (v + NL) % IDS
            eng.dma_start(ids_b[:, slot, :], ids_t[f:f + 1, bass.ds(at, HS)].to_broadcast([LP, HS])).then_inc(s_ids[slot], 16)

        def next_ids(eng, c, v):
            eng.wait_ge(s_mask[1], lookups(c, v) - IDS + 1)
            eng.sem_inc(s_load_open, 1)
            load_ids(eng, c, v)

        def load_dense(sp, c, h):
            sp.dma_start(dense_x[:], dense_t[:, bass.ds(c * CS + h * HS, HS)]).then_inc(s_dense, 16)

        def half_in_gram(eng, c, h):
            for r in ((h + 1) * HALF * ROUNDS - 2, (h + 1) * HALF * ROUNDS - 1):
                eng.wait_ge(s_gram_act[r % 2], half_rounds(c, r) + 2)
                eng.wait_ge(s_gram_dve[r % 2], half_rounds(c, r) + 2)
                eng.sem_inc(s_load_open, 1)

        def gram_row(h, half_j):
            return (half_j * 2 + h) * QUAD

        def pairs_of(h, j):
            t, z = PLACE[j]
            p0 = gram_row(h, (j - 1) // GG)
            return pairs[z:z + j, t, :], gram[p0:p0 + j, (j - 1) % GG, :]

        def lay_out_pairs(eng, h, js, done):
            for j in js:
                place, products = pairs_of(h, j)
                eng.dma_start(place, products).then_inc(done, 16)

        def copy_pairs(name, eng, copy, c, h, n):
            if n == 0:
                half_in_gram(eng, c, h)
                if not (in_first(c) and h == 0):
                    eng.wait_ge(s_split, splits(c, h, K1 - SPLITS))
            for j in COPIED[(0 if name == "act" else 1)::2][n::COPY_STEPS]:
                last = copy(*pairs_of(h, j))
            last.then_inc(s_copied[name], 1)

        def copies(c, h):
            return c * (2 * COPY_STEPS) + (h + 1) * COPY_STEPS

        def open_pairs(eng, c, h):
            half_in_gram(eng, c, h)
            if not (in_first(c) and h == 0):
                eng.wait_ge(s_split, splits(c, h, K1 - SPLITS))
                eng.sem_inc(s_load_open, 1)

        def store_scores(sp, c, h):
            sp.wait_ge(s_taken[bank(h, L30)], shared_uses(c, h, L30) + 2)
            sp.sem_inc(s_load_open, 1)
            sp.dma_start(y[bass.ds(c * CS + h * HS, HS), :].rearrange("s o -> o s"), y_row).then_inc(s_out, 16)

        def pairs_laid_out(eng, c, h):
            if in_last(c) and h == 1:
                eng.wait_ge(s_pairs[h], c * (len(BY_DMA) * 16) + len(LAST_SP) * 16)
                eng.wait_ge(s_pairs_pool, len(LAST_POOL) * 16)
            else:
                eng.wait_ge(s_pairs[h], (c + 1) * (len(BY_DMA) * 16))
            for name in s_copied:
                eng.wait_ge(s_copied[name], copies(c, h))

        block = ctx.enter_context(nc.Block())

        @block.sync
        def _(sp):
            def load_table(i):
                f = LF[i]
                for p0, p1 in ((0, 112), (112, LP)):
                    sp.dma_start(table_arrives(f)[p0:p1, :],
                                 tables[f].rearrange("(p k) d -> p (k d)", p=LP)[p0:p1, :]).then_inc(s_table[i], 16)

            for k in range(TILES):
                sp.dma_start(idx[:, k, :], ids[k * P:(k + 1) * P, :]).then_inc(s_idx[k], 16)
                if k == 0:
                    for v in range(IDS):
                        load_ids(sp, 0, v - NL)
                load_table(k)
            for i in range(TILES, NL):
                load_table(i)
            load_dense(sp, 0, 0)
            sp.dma_start(w1z_in, w1z).then_inc(s_weights, 16)
            sp.dma_start(w1d_in, w1[PAIRS:PAIRS + D, :]).then_inc(s_weights, 16)
            sp.dma_start(w2_in.rearrange("p (c n) -> p c n", c=N1),
                         w2.rearrange("(c p) n -> p c n", p=P)).then_inc(s_weights, 16)
            with nc.allow_non_contiguous_dma(reason="small vectors, one value per partition"):
                sp.dma_start(w3s[:], w3.rearrange("(c p) o -> p (c o)", p=P)).then_inc(s_weights, 16)
                sp.dma_start(b1s[:], b1.rearrange("(c p) -> p c", p=P)).then_inc(s_weights, 16)
                sp.dma_start(b2s[:], b2.rearrange("(c p) -> p c", p=P)).then_inc(s_weights, 16)
            for v in range(IDS - NL, IDS):
                next_ids(sp, 0, v)

            def chunk(c):
                for k in range(TILES):
                    pairs_now = k % HALF == 0 and not (in_first(c) and k == 0)
                    if pairs_now:
                        before = half_before(c, k)
                        open_pairs(sp, *before)
                    loads = [v + IDS for v, e in lookup_halves(c, k) if e == 0 and not (in_last(c) and v + IDS >= NL)]
                    for at in range(0, len(BY_DMA), PAIRS_STEP):
                        if pairs_now:
                            lay_out_pairs(sp, before[1], BY_DMA[at:at + PAIRS_STEP], s_pairs[before[1]])
                        if loads:
                            next_ids(sp, c, loads.pop(0))
                    if k % HALF == 0 and not (in_first(c) and k <= HALF):
                        store_scores(sp, *half_before(before[0], before[1] * HALF))
                    if not in_last(c):
                        sp.wait_ge(s_gathered[k % 2], (slot_tiles(c, k) + 1) * (16 * NG))
                        sp.sem_inc(s_load_open, 1)
                        sp.dma_start(idx[:, k, :], ids[bass.ds((c + 1) * CS + k * P, P), :]).then_inc(s_idx[k], 16)
                    if k % HALF == 0 and not (in_last(c) and k >= HALF):
                        sp.wait_ge(s_dense_used, c * 2 + (k // HALF + 1))
                        sp.sem_inc(s_load_open, 1)
                        load_dense(sp, c, k // HALF + 1)

            chunk(0)
            with sp.Fori(1, CHUNKS - 1) as c:
                chunk(c)
            chunk(CHUNKS - 1)
            open_pairs(sp, CHUNKS - 1, 1)
            lay_out_pairs(sp, 1, LAST_SP, s_pairs[1])
            store_scores(sp, CHUNKS - 1, 0)
            store_scores(sp, CHUNKS - 1, 1)
            sp.wait_ge(s_out, 16 * (2 * CHUNKS + 1))

        @block.gpsimd
        def _(pool):
            pool.memset(ident[:], 0.0).then_inc(s_zero, 1)
            pool.wait_ge(s_zero, 1)
            pool.affine_select(out=ident[:], in_=ident[:], compare_op=ALU.not_equal, fill=1.0, base=0,
                               pattern=[[-1, P]], channel_multiplier=1).then_inc(s_ident, 1)
            for n, i in row_kind.items():
                last = pool.iota(row_int[:, i, 0:n], pattern=[[1, n]], base=0, channel_multiplier=n)
            last.then_inc(s_row_int, 1)

            def chunk(c):
                for k in range(TILES):
                    pool.wait_ge(s_idx[k], (c + 1) * 16)
                    pool.wait_ge(s_turned[k % 2], turned(c, k, 0))
                    pool.sem_inc(s_tile_open, 1)
                    for slot, f in enumerate(ROWS):
                        pool.indirect_dma_start(
                            rows[:, k % 2, slot, :], None, tables[f],
                            bass.IndirectOffsetOnAxis(ap=idx[:, k, f:f + 1], axis=0),
                        ).then_inc(s_last_rows[slot // TURN] if in_last_tile(c, k) else s_gathered[k % 2], 16)

            with pool.Fori(0, CHUNKS - 1) as c:
                chunk(c)
            chunk(CHUNKS - 1)
            open_pairs(pool, CHUNKS - 1, 1)
            lay_out_pairs(pool, 1, LAST_POOL, s_pairs_pool)

        @block.tensor
        def _(pe):
            def turn(c, k, i):
                if in_last_tile(c, k):
                    pe.wait_ge(s_last_rows[i], 16 * len(TURNS[i]))
                elif i == 0:
                    pe.wait_ge(s_gathered[k % 2], (slot_tiles(c, k) + 1) * (16 * NG))
                two = in_last(c) and k >= HALF and i > 0
                if two:
                    pe.wait_ge(s_look_taken, lookups(c, NL) + 1)
                pe.wait_ge(s_xt, batches(c, k, i - 1 if two else i))
                for j, f in enumerate(TURNS[i]):
                    last = nc.tensor.transpose(turn_bank(c, k, i)[:, j * P:(j + 1) * P],
                                               rows[:, k % 2, ROWS.index(f), :], ident[:])
                last.then_inc(s_turned[k % 2], 1)

            def look_up(c, v, e):
                f = LF[v % NL]
                if e == 0:
                    pe.wait_ge(s_look_taken, lookups(c, v) + 1)
                pe.wait_ge(s_mask[e], lookups(c, v) + 1)
                for k in range(PART[f]):
                    for part in range(2):
                        first = e == 0 and k == 0 and part == 0
                        stop = e == 1 and k == PART[f] - 1 and part == 1
                        last = nc.tensor.matmul(look_ps[:, 0:HS],
                                                (table_hi, table_lo)[part][:, table_at[f] + e * PART[f] + k, :],
                                                masks[:, e, k, :],
                                                start=first, stop=stop)
                last.then_inc(s_look if e else s_mask_used, 1)

            def products(c, k, i):
                if i == 0:
                    if in_first(c) and k == 0:
                        pe.wait_ge(s_pads, 2)
                    pe.wait_ge(s_xt, batches(c, k, BATCHES))
                    if k % HALF == 0:
                        pe.wait_ge(s_look_taken, lookups(c, k // HALF * NL) + 1)
                r = k * ROUNDS + i
                pe.wait_ge(s_gram_act[r % 2], half_rounds(c, r) + 1)
                pe.wait_ge(s_gram_dve[r % 2], half_rounds(c, r) + 1)
                for j in range(ROUND):
                    grp = i * ROUND + j
                    last = nc.tensor.matmul(gram_ps[:, r % 2, j, 0:Q * NF],
                                            xt[:, k, grp * Q:(grp + 1) * Q, :].rearrange("p q f -> p (q f)"),
                                            xt[:, k, grp * Q:(grp + 1) * Q, 1:NV], start=True, stop=True)
                last.then_inc(s_gram[r % 2], 1)

            def split_products(out, weights, values, start, stop):
                (w_hi, w_lo), (x_hi, x_lo) = weights, values
                nc.tensor.matmul(out, w_hi, x_hi, start=start, stop=False)
                nc.tensor.matmul(out, w_hi, x_lo, start=False, stop=False)
                return nc.tensor.matmul(out, w_lo, x_hi, start=False, stop=stop)

            def layer1(c, h, n):
                if n == 0:
                    if in_first(c) and h == 0:
                        pe.wait_ge(s_w_lo, 3)
                at = slice(n * P, (n + 1) * P)
                for i, t in enumerate((KZ, *range(KZ))):
                    if n == 0:
                        pe.wait_ge(s_split, splits(c, h, i + 1))
                    last = split_products(shared_ps[:, bank(h, n), 0:HS], (w1_hi[:, t, at], w1_lo[:, t, at]),
                                          (z_hi[:, t, :], z_lo[:, t, :]), i == 0, i == KZ)
                return last

            def layer2(c, h, n):
                at = slice(n * P, (n + 1) * P)
                for t in range(N1):
                    if n == 0:
                        pe.wait_ge(s_split, splits(c, h, K1 + t + 1))
                    last = split_products(shared_ps[:, bank(h, L20 + n), 0:HS], (w2_hi[:, t, at], w2_lo[:, t, at]),
                                          (h_hi[:, t, :], h_lo[:, t, :]), t == 0, t == N1 - 1)
                return last

            def layer3(c, h):
                taken(pe, c, h, L30 - 1)
                for t in range(N2):
                    last = nc.tensor.matmul(shared_ps[0:1, bank(h, L30), 0:HS], w3s[:, t:t + 1], h2[:, t, :],
                                            start=(t == 0), stop=(t == N2 - 1))
                return last

            def end_step(c, h, u):
                pe.wait_ge(s_taken[bank(h, u)], shared_uses(c, h, u) + 1)
                if u < L20:
                    last = layer1(c, h, u)
                elif u < L30:
                    last = layer2(c, h, u - L20)
                else:
                    last = layer3(c, h)
                last.then_inc(s_shared[bank(h, u)], 1)

            for slot in range(2):
                pe.sem_inc(s_turned[slot], 1)
            pe.wait_ge(s_ident, 1)
            for kind, n in first_steps():
                if kind == "T":
                    turn(0, 0, n)
                else:
                    v, e = divmod(n, 2)
                    pe.wait_ge(s_table_lo, v + 1)
                    look_up(0, v - NL, e)

            def chunk(c):
                for k in range(TILES):
                    for kind, n, e in tile_steps(c, k):
                        if kind == "T":
                            turn(c, k, n)
                        elif kind == "L":
                            look_up(c, n, e)
                        elif kind == "G":
                            products(c, k, n)
                        elif kind == "E":
                            end_step(*half_before(c, k), n)

            chunk(0)
            with pe.Fori(1, CHUNKS - 1) as c:
                chunk(c)
            chunk(CHUNKS - 1)
            for kind, n, h in final_steps():
                if kind == "E":
                    end_step(CHUNKS - 1, h, n)

        def take_round(eng, copy, c, k, i, quads, done):
            r = k * ROUNDS + i
            if in_first(c) and r == 0:
                eng.wait_ge(s_no_pairs, 1)
                eng.wait_ge(s_w_lo, 3)
            if k % HALF == 0 and i == 0 and not in_first(c):
                eng.wait_ge(s_pairs[k // HALF], c * (len(BY_DMA) * 16))
                for name in s_copied:
                    eng.wait_ge(s_copied[name], copies(c, k // HALF) - 2 * COPY_STEPS)
            eng.wait_ge(s_gram[r % 2], half_rounds(c, r) + 1)
            for q in quads:
                p0 = q * QUAD
                for half_j in range(2):
                    to, at = gram_row(k // HALF, half_j), q * NF + half_j * GG
                    samples = bass.ds(k % HALF * P + i * ROUND * Q + q, ROUND, Q)
                    last = copy(gram[to:to + NF, :, samples].rearrange("p g s -> p s g"),
                                gram_ps[p0:p0 + NF, r % 2, :, at:at + GG])
            last.then_inc(done[r % 2], 1)

        @block.scalar
        def _(act):
            act.sem_inc(s_xt, 1)
            act.sem_inc(s_look_taken, 1)
            for b in range(2):
                act.sem_inc(s_gram_act[b], 1)
                act.sem_inc(s_taken[b], 1)
            act.sem_inc(s_out, 16)

            def take_batch(c, k, i):
                act.wait_ge(s_turned[k % 2], turned(c, k, i + 1))
                if k % HALF == 0 and i == 0:
                    h = k // HALF
                    act.wait_ge(s_dense, c * 32 + (h + 1) * 16)
                    nc.scalar.copy(xt[:, k:k + HALF, :, NF],
                                   dense_x[:].rearrange("p (k s) -> p k s", k=HALF)).then_inc(s_dense_used, 1)
                for at, f, step, n in runs(TURNS[i]):
                    last = nc.scalar.copy(xt[:, k, :, f:f + (n - 1) * step + 1:step].rearrange("p s f -> p f s"),
                                          turn_bank(c, k, i)[:, at * P:(at + n) * P].rearrange("p (f s) -> p f s", f=n))
                last.then_inc(s_xt, 1)

            def take_lookup(c, v):
                k = 0 if v < 0 or v >= NL else HALF
                if in_first(c) and v == 0:
                    act.wait_ge(s_table_lo, NL)
                act.wait_ge(s_look, lookups(c, v) + 1)
                nc.scalar.copy(xt[:, k:k + HALF, :, LF[v % NL]],
                               look_ps[:, 0:HS].rearrange("p (k s) -> p k s", k=HALF)).then_inc(s_look_taken, 1)

            def upper_table(i):
                f = LF[i]
                act.wait_ge(s_table[i], 32)
                at, n = table_at[f], LOOKED[f]
                nc.scalar.copy(table_hi[:, at:at + n, :].rearrange("p k d -> p (k d)"), table_arrives(f)).then_inc(s_table_hi, 1)

            for i in range(2):
                upper_table(i)
            for kind, n in first_steps():
                if kind == "T":
                    take_batch(0, 0, n)
                elif n % 2 == 0 and n // 2 + 2 < NL:
                    upper_table(n // 2 + 2)
                elif n % 2 == 1:
                    take_lookup(0, n // 2 - NL)
            act.wait_ge(s_weights, 16 * 6)
            nc.scalar.copy(w1_hi[:, 0:KZ, :], w1z_in).then_inc(s_w_hi, 1)
            nc.scalar.copy(w1_hi[:, KZ, :], w1d_in).then_inc(s_w_hi, 1)
            nc.scalar.copy(w2_hi[:, :, :].rearrange("p c n -> p (c n)"), w2_in).then_inc(s_w_hi, 1)

            def upper_part(c, h, t):
                if t < KZ:
                    pairs_laid_out(act, c, h)
                    nc.scalar.copy(z_hi[:, t, :], pairs[:, t, :]).then_inc(s_pairs_upper, 1)

            def end_step(c, h, u):
                b = bank(h, u)
                shared_done(act, c, h, u)
                if u < L20:
                    if u == 1:
                        act.wait_ge(s_out, c * 32 + (h + 1) * 16)
                    if u >= 2:
                        act.wait_ge(s_split, splits(c, h, K1 + u - 1))
                    last = nc.scalar.activation(whole[:, u % 2, :], shared_ps[:, b, 0:HS], ACT.Relu, bias=b1s[:, u:u + 1])
                elif u < L30:
                    n = u - L20
                    last = nc.scalar.activation(h2[:, n, :], shared_ps[:, b, 0:HS], ACT.Relu, bias=b2s[:, n:n + 1])
                else:
                    last = nc.scalar.copy(y_row, shared_ps[0:1, b, 0:HS])
                last.then_inc(s_taken[b], 1)

            def chunk(c):
                for k in range(TILES):
                    for kind, n, e in tile_steps(c, k):
                        if kind == "T":
                            take_batch(c, k, n)
                        elif kind == "L" and e == 1:
                            take_lookup(c, n)
                        elif kind == "C":
                            copy_pairs("act", act, nc.scalar.copy, *half_before(c, k), n)
                        elif kind == "S":
                            upper_part(*half_before(c, k), n)
                        elif kind == "G":
                            take_round(act, nc.scalar.copy, c, k, n, (0, 1, 2), s_gram_act)
                        elif kind == "E":
                            end_step(*half_before(c, k), n)

            chunk(0)
            with act.Fori(1, CHUNKS - 1) as c:
                chunk(c)
            chunk(CHUNKS - 1)
            for kind, n, h in final_steps():
                if kind == "C":
                    copy_pairs("act", act, nc.scalar.copy, CHUNKS - 1, h, n)
                elif kind == "S":
                    upper_part(CHUNKS - 1, h, n)
                else:
                    end_step(CHUNKS - 1, h, n)

        @block.vector
        def _(dve):
            for b in range(2):
                dve.sem_inc(s_gram_dve[b], 1)
            dve.wait_ge(s_row_int, 1)
            for n, i in row_kind.items():
                last = nc.vector.tensor_copy(row_no[:, i, 0:n], row_int[:, i, 0:n])
            last.then_inc(s_row_no, 1)
            dve.wait_ge(s_row_no, 1)

            def lower(lo, whole_, hi):
                return nc.vector.tensor_tensor(lo, whole_, hi.bitcast(F32), ALU.subtract)

            def mask(c, v, e):
                f = LF[v % NL]
                slot = (v + NL) % IDS
                if e == 0:
                    dve.wait_ge(s_ids[slot], ids_value(c, v))
                if v > -NL:
                    dve.wait_ge(s_look if e else s_mask_used, lookups(c, v))
                for k in range(PART[f]):
                    at = e * PART[f] + k
                    last = nc.vector.tensor_scalar(masks[:, e, k, :], ids_b[:, slot, :],
                                                   row_no[:, row_kind[LOOKED[f]], at:at + 1], None, ALU.is_equal)
                last.then_inc(s_mask[e], 1)

            def lower_table(i):
                f = LF[i]
                dve.wait_ge(s_table[i], 32)
                dve.wait_ge(s_table_hi, i + 1)
                at, n = table_at[f], LOOKED[f]
                lower(table_lo[:, at:at + n, :].rearrange("p k d -> p (k d)"), table_arrives(f),
                      table_hi[:, at:at + n, :].rearrange("p k d -> p (k d)")).then_inc(s_table_lo, 1)

            nc.vector.memset(pairs[:], 0.0).then_inc(s_no_pairs, 1)
            nc.vector.memset(xt[:, 0:HALF, :, NV:QUAD], 0.0).then_inc(s_pads, 1)
            for i in range(NL):
                mask(0, i - NL, 0)
                lower_table(i)
                mask(0, i - NL, 1)
            for e in range(2):
                mask(0, 0, e)
            dve.wait_ge(s_weights, 16 * 6)
            dve.wait_ge(s_w_hi, 3)
            lower(w1_lo[:, 0:KZ, :], w1z_in, w1_hi[:, 0:KZ, :]).then_inc(s_w_lo, 1)
            lower(w1_lo[:, KZ, :], w1d_in, w1_hi[:, KZ, :]).then_inc(s_w_lo, 1)
            lower(w2_lo[:, :, :].rearrange("p c n -> p (c n)"), w2_in,
                  w2_hi[:, :, :].rearrange("p c n -> p (c n)")).then_inc(s_w_lo, 1)
            dve.wait_ge(s_table_lo, NL)
            nc.vector.memset(xt[:, HALF:TILES, :, NV:QUAD], 0.0).then_inc(s_pads, 1)

            def split(c, h, n, hi, lo, whole_):
                nc.vector.tensor_copy(hi, whole_).then_inc(s_upper, 1)
                dve.wait_ge(s_upper, c * (2 * (1 + N1)) + h * (1 + N1) + (n + 1))
                lower(lo, whole_, hi).then_inc(s_split, 1)

            def split_input(c, h, t):
                if t == KZ:
                    def by_tile(x):
                        return x.rearrange("p (k s) -> p k s", k=HALF)
                    split(c, h, 0, by_tile(z_hi[:, t, :]), by_tile(z_lo[:, t, :]),
                          xt[:, h * HALF:(h + 1) * HALF, :, NF])
                else:
                    pairs_laid_out(dve, c, h)
                    dve.wait_ge(s_pairs_upper, c * (2 * KZ) + (h * KZ + t + 1))
                    lower(z_lo[:, t, :], pairs[:, t, :], z_hi[:, t, :]).then_inc(s_split, 1)

            def end_step(c, h, u):
                if u < L20:
                    dve.wait_ge(s_taken[bank(h, u)], shared_uses(c, h, u) + 2)
                    split(c, h, 1 + u, h_hi[:, u, :], h_lo[:, u, :], whole[:, u % 2, :])

            def chunk(c):
                for k in range(TILES):
                    for kind, n, e in tile_steps(c, k):
                        if kind == "L":
                            v1, e1 = divmod(2 * n + e + 2, 2)
                            if not (in_last(c) and v1 >= NL):
                                mask(c, v1, e1)
                        elif kind == "C":
                            copy_pairs("dve", dve, nc.vector.tensor_copy, *half_before(c, k), n)
                        elif kind == "S":
                            split_input(*half_before(c, k), n)
                        elif kind == "G":
                            take_round(dve, nc.vector.tensor_copy, c, k, n, (3,), s_gram_dve)
                        elif kind == "E":
                            end_step(*half_before(c, k), n)

            chunk(0)
            with dve.Fori(1, CHUNKS - 1) as c:
                chunk(c)
            chunk(CHUNKS - 1)
            for kind, n, h in final_steps():
                if kind == "C":
                    copy_pairs("dve", dve, nc.vector.tensor_copy, CHUNKS - 1, h, n)
                elif kind == "S":
                    split_input(CHUNKS - 1, h, n)
                else:
                    end_step(CHUNKS - 1, h, n)


_INS = ["ids"] + [f"tbl_{f}" for f in range(NF)] + ["W_top1", "b_top1", "W_top2", "b_top2", "W_top3"]


def kernel(**inputs):
    import numpy as np
    import concourse.bacc as bacc
    from concourse.bass_utils import run_bass_kernel_spmd as run

    nc = bacc.Bacc("TRN2", target_bir_lowering=False, num_devices=1)
    given = {name: inputs[name] for name in _INS}
    given["dense_t"] = inputs["r_dense_x"].T
    given["ids_t"] = inputs["ids"].T
    given["w1z"] = np.zeros((P, KZ, H1), inputs["W_top1"].dtype)
    for j, (t, z) in PLACE.items():
        given["w1z"][z:z + j, t, :] = inputs["W_top1"][[f * NV - f * (f + 1) // 2 + j - f - 1 for f in range(j)], :]
    arrays, a = {}, {}
    for name, x in given.items():
        x = np.ascontiguousarray(x)
        arrays[f"in_{name}"] = x
        a[name] = nc.dram_tensor(f"in_{name}", x.shape, mybir.dt.from_np(x.dtype), kind="ExternalInput").ap()
    y = nc.dram_tensor("out_y", (B, 1), F32, kind="ExternalOutput").ap()
    build(nc, a["dense_t"], a["ids"], a["ids_t"], [a[f"tbl_{f}"] for f in range(NF)], a["w1z"], a["W_top1"], a["b_top1"],
          a["W_top2"], a["b_top2"], a["W_top3"], y)
    r = run(nc, [arrays], core_ids=[0])
    return r.results[0]["out_y"]
```
